# Optimizing a Trainium2 kernel written in Bass

```python
import numpy as np
import jax
import jax.numpy as jnp

def _softmax(x, axis=-1):
    return jax.nn.softmax(x, axis=axis)

def _gelu(x):
    return jax.nn.gelu(x, approximate=True)

def _silu(x):
    return jax.nn.silu(x)

def _sigmoid(x):
    return jax.nn.sigmoid(x)

def _layernorm(x, axis=-1, eps=1e-05):
    m = jnp.mean(x, axis=axis, keepdims=True)
    v = jnp.var(x, axis=axis, keepdims=True)
    return (x - m) / jnp.sqrt(v + eps)

def _scatter_add(tgt, idx, src, axis=0):
    return tgt.at[idx].add(src)

def _segment_sum(src, seg, n):
    return jax.ops.segment_sum(src, seg, n)
kernel_name = 'mk_rec_standalone_d1_rec_r8_469b24'

def setup_inputs(seed: int=0):
    np.random.seed(seed)
    _w = jnp.asarray

    def _rec_inputs():
        import jax
        import jax.numpy as jnp
        _rk = jax.random.key(seed)
        r_dense = -0.00338568 + 1.0005 * jax.random.normal(jax.random.fold_in(_rk, 1), (2048, 13), jnp.float32)
        r_sparse = jnp.stack([jax.random.randint(jax.random.fold_in(jax.random.fold_in(_rk, 2), 0), (2048,), 2, 12500, jnp.int32), jax.random.randint(jax.random.fold_in(jax.random.fold_in(_rk, 2), 1), (2048,), 1, 99999, jnp.int32), jax.random.randint(jax.random.fold_in(jax.random.fold_in(_rk, 2), 2), (2048,), 0, 12500, jnp.int32), jax.random.randint(jax.random.fold_in(jax.random.fold_in(_rk, 2), 3), (2048,), 5, 12500, jnp.int32), jax.random.randint(jax.random.fold_in(jax.random.fold_in(_rk, 2), 4), (2048,), 20, 99993, jnp.int32), jax.random.randint(jax.random.fold_in(jax.random.fold_in(_rk, 2), 5), (2048,), 0, 99993, jnp.int32), jax.random.randint(jax.random.fold_in(jax.random.fold_in(_rk, 2), 6), (2048,), 2, 99999, jnp.int32), jax.random.randint(jax.random.fold_in(jax.random.fold_in(_rk, 2), 7), (2048,), 2, 99995, jnp.int32), jax.random.randint(jax.random.fold_in(jax.random.fold_in(_rk, 2), 8), (2048,), 0, 99999, jnp.int32), jax.random.randint(jax.random.fold_in(jax.random.fold_in(_rk, 2), 9), (2048,), 2, 99986, jnp.int32), jax.random.randint(jax.random.fold_in(jax.random.fold_in(_rk, 2), 10), (2048,), 4, 99999, jnp.int32), jax.random.randint(jax.random.fold_in(jax.random.fold_in(_rk, 2), 11), (2048,), 15, 99999, jnp.int32), jax.random.randint(jax.random.fold_in(jax.random.fold_in(_rk, 2), 12), (2048,), 0, 99989, jnp.int32), jax.random.randint(jax.random.fold_in(jax.random.fold_in(_rk, 2), 13), (2048,), 5, 99990, jnp.int32), jax.random.randint(jax.random.fold_in(jax.random.fold_in(_rk, 2), 14), (2048,), 2, 99996, jnp.int32), jax.random.randint(jax.random.fold_in(jax.random.fold_in(_rk, 2), 15), (2048,), 3, 99994, jnp.int32), jax.random.randint(jax.random.fold_in(jax.random.fold_in(_rk, 2), 16), (2048,), 0, 99998, jnp.int32), jax.random.randint(jax.random.fold_in(jax.random.fold_in(_rk, 2), 17), (2048,), 13, 99998, jnp.int32), jax.random.randint(jax.random.fold_in(jax.random.fold_in(_rk, 2), 18), (2048,), 10, 12498, jnp.int32), jax.random.randint(jax.random.fold_in(jax.random.fold_in(_rk, 2), 19), (2048,), 0, 99999, jnp.int32), jax.random.randint(jax.random.fold_in(jax.random.fold_in(_rk, 2), 20), (2048,), 0, 99995, jnp.int32), jax.random.randint(jax.random.fold_in(jax.random.fold_in(_rk, 2), 21), (2048,), 1, 99998, jnp.int32), jax.random.randint(jax.random.fold_in(jax.random.fold_in(_rk, 2), 22), (2048,), 1, 99997, jnp.int32), jax.random.randint(jax.random.fold_in(jax.random.fold_in(_rk, 2), 23), (2048,), 2, 99989, jnp.int32), jax.random.randint(jax.random.fold_in(jax.random.fold_in(_rk, 2), 24), (2048,), 6, 12500, jnp.int32), jax.random.randint(jax.random.fold_in(jax.random.fold_in(_rk, 2), 25), (2048,), 2, 99995, jnp.int32)], axis=1)
        return (r_dense, r_sparse)
    r_dense, r_sparse = _rec_inputs()

    def _L0_rec_setup():
        import jax, jax.numpy as jnp
        import numpy as np
        B, N_DENSE, N_FIELDS, VOCAB, EMBED_DIM, ATT_DIM = (2048, 13, 26, 12500, 32, 8)
        FIRST, SECOND = np.triu_indices(N_FIELDS, k=1)
        key = jax.random.key(seed)
        ks = jax.random.split(key, 8)
        dense = jax.random.normal(ks[0], (B, N_DENSE), dtype=jnp.float32)
        sparse = jax.random.randint(ks[1], (B, N_FIELDS), 0, VOCAB, dtype=jnp.int32)
        s = 1.0 / np.sqrt(EMBED_DIM)
        embed_tables = jax.random.normal(ks[2], (N_FIELDS, VOCAB, EMBED_DIM), dtype=jnp.float32) * 0.01
        att_w_w = jax.random.normal(ks[3], (EMBED_DIM, ATT_DIM), dtype=jnp.float32) * s
        att_w_b = jnp.zeros((ATT_DIM,), dtype=jnp.float32)
        att_d_w = jax.random.normal(ks[4], (ATT_DIM, 1), dtype=jnp.float32) * (1.0 / np.sqrt(ATT_DIM))
        att_d_b = jnp.zeros((1,), dtype=jnp.float32)
        fin_w = jax.random.normal(ks[5], (EMBED_DIM + N_DENSE, 1), dtype=jnp.float32) * 0.05
        fin_b = jnp.zeros((1,), dtype=jnp.float32)
        return {'dense': dense, 'sparse': sparse, 'embed_tables': embed_tables, 'att_w_w': att_w_w, 'att_w_b': att_w_b, 'att_d_w': att_d_w, 'att_d_b': att_d_b, 'fin_w': fin_w, 'fin_b': fin_b}
    _L0_rec_all = _L0_rec_setup()
    _L0_rec_in = {k: v for k, v in _L0_rec_all.items() if k in ('embed_tables', 'att_w_w', 'att_w_b', 'att_d_w', 'att_d_b', 'fin_w', 'fin_b')}
    del _L0_rec_all
    return {'r_dense': r_dense, 'r_sparse': r_sparse, 'L0_rec_embed_tables': _L0_rec_in['embed_tables'], 'L0_rec_att_w_w': _L0_rec_in['att_w_w'], 'L0_rec_att_w_b': _L0_rec_in['att_w_b'], 'L0_rec_att_d_w': _L0_rec_in['att_d_w'], 'L0_rec_att_d_b': _L0_rec_in['att_d_b'], 'L0_rec_fin_w': _L0_rec_in['fin_w'], 'L0_rec_fin_b': _L0_rec_in['fin_b']}

def reference(r_dense, r_sparse, L0_rec_embed_tables, L0_rec_att_w_w, L0_rec_att_w_b, L0_rec_att_d_w, L0_rec_att_d_b, L0_rec_fin_w, L0_rec_fin_b):
    import jax
    import jax.numpy as jnp

    def _L0_rec_ref(dense, sparse, embed_tables, att_w_w, att_w_b, att_d_w, att_d_b, fin_w, fin_b):
        import jax, jax.numpy as jnp
        import numpy as np
        B, N_DENSE, N_FIELDS, VOCAB, EMBED_DIM, ATT_DIM = (2048, 13, 26, 12500, 32, 8)
        FIRST, SECOND = np.triu_indices(N_FIELDS, k=1)
        emb = jax.vmap(lambda tbl, idx: tbl[idx], in_axes=(0, 1), out_axes=1)(embed_tables, sparse)
        bi = emb[:, FIRST, :] * emb[:, SECOND, :]
        a = jax.nn.relu(jnp.einsum('bpd,dh->bph', bi, att_w_w) + att_w_b)
        scores = jnp.einsum('bph,ho->bpo', a, att_d_w) + att_d_b
        att_weight = jax.nn.softmax(scores, axis=1)
        att_out = jnp.sum(att_weight * bi, axis=1)
        x = jnp.concatenate([att_out, dense], axis=-1)
        out = jax.nn.sigmoid(x @ fin_w + fin_b)
        return out.reshape(out.shape[0])
    y = _L0_rec_ref(r_dense, r_sparse, L0_rec_embed_tables, L0_rec_att_w_w, L0_rec_att_w_b, L0_rec_att_d_w, L0_rec_att_d_b, L0_rec_fin_w, L0_rec_fin_b)
    return y

_drawn_inputs = setup_inputs


def setup_inputs(seed=0):
    import zlib

    import numpy as np

    out = dict(_drawn_inputs(seed))
    spreads = {'L0_rec_att_w_b': (0.0, 2.0)}
    factors = {'L0_rec_embed_tables': 64.0, 'L0_rec_att_d_w': 64.0, 'L0_rec_att_w_w': 8.0}
    for name, (base, spread) in spreads.items():
        noise = np.random.default_rng([zlib.crc32(name.encode()), seed]).standard_normal(out[name].shape)
        drawn = base * np.exp(spread * noise) if base else spread * noise
        out[name] = jnp.asarray(drawn.astype(out[name].dtype))
    for name, factor in factors.items():
        out[name] = (out[name] * factor).astype(out[name].dtype)
    return out
```

```python
from contextlib import ExitStack

import concourse.bass as bass
from concourse import mybir

P = 128
G = 4
COL_TILES = 2
PAIRS_C = 4
PAIRS_G = COL_TILES * PAIRS_C
ROWS_C = P // COL_TILES
OUTS = 2
ROWS_G = OUTS * G * COL_TILES
GROUPS_B = P // ROWS_G
RING = 16
SLOTS = 13
MASKED = -3.0e38


def layout(n_fields, embed_dim, att_dim, n_dense):
    at, cols = 0, {}
    for name, width in (("offset", n_fields), ("w", ROWS_C), ("sign", ROWS_C), ("d", 2 * 32), ("bias_a", 1),
                        ("bias_s", 1), ("dense_w", n_dense), ("fin_b", 1), ("ident", P)):
        cols[name] = slice(at, at + width)
        at += width
    return cols, at


def attention_fm(nc, dense, sparse, tables, params, out):
    f32, i32 = mybir.dt.float32, mybir.dt.int32
    ALU, ACT, AX = mybir.AluOpType, mybir.ActivationFunctionType, mybir.AxisListType

    B, F = sparse.shape
    V, D = tables.shape[1:]
    N_DENSE = dense.shape[1]
    T = B // P
    QUADS = T // G
    STEPS = QUADS * F
    CYCLES = STEPS // SLOTS
    PAIRS = F * (F - 1) // 2
    GROUPS = -(-PAIRS // PAIRS_G)
    BANKS = -(-GROUPS // GROUPS_B)
    FULL = BANKS - 1
    BLOCKS = FULL * PAIRS_C * GROUPS_B + PAIRS_C
    assert G * D == P and B % (P * G) == 0 and F % SLOTS == 0 and GROUPS == FULL * GROUPS_B + 1
    assert PAIRS - (GROUPS - 1) * PAIRS_G == PAIRS_C + 1 and RING < GROUPS

    pieces = []
    for f in range(F):
        a, end = f * (f - 1) // 2, f * (f + 1) // 2
        while a < end:
            b = min(end, (a // PAIRS_G + 1) * PAIRS_G)
            pieces.append((f, a, b))
            a = b
    PIECES = len(pieces)

    def pieces_before_field(f):
        return sum(1 for piece in pieces if piece[0] < f)

    def pieces_through_group(g):
        return sum(1 for piece in pieces if piece[1] < (g + 1) * PAIRS_G)

    def groups_of(f):
        first, end = f * (f - 1) // 2 // PAIRS_G, f * (f + 1) // 2 // PAIRS_G
        return list(range(first, GROUPS if f == F - 1 else end)) if f else []

    cols, _ = layout(F, D, 0, N_DENSE)

    ctx = ExitStack()
    with ctx:
        def sb(name, shape, dt=f32):
            return ctx.enter_context(nc.sbuf_tensor(name, shape, dt))

        def psum(name, shape):
            return ctx.enter_context(nc.psum_tensor(name, shape, f32))

        def sem(name):
            return ctx.enter_context(nc.semaphore(name))

        par = sb("par", [P, params.shape[1]])
        ids = sb("ids", [P, T, F], i32)
        clamped = sb("clamped", [P, T, F])
        wrap = sb("wrap", [P, T, F])
        wrapped = sb("wrapped", [P, T, F])
        rows = sb("rows", [P, STEPS + SLOTS, G], i32)
        row_slot = sb("row_slot", [P, SLOTS, G], i32)
        emb = sb("emb", [P, SLOTS, G * D])
        emb_t = sb("emb_t", [P, F, P])
        ring = sb("ring", [P, RING, PAIRS_G, P])
        w_block = sb("w_block", [P, ROWS_C])
        hidden = sb("hidden", [P, 3, PAIRS_C * P])
        second = sb("second", [P, 2, PAIRS_C * P])
        result = sb("result", [P, BLOCKS, ROWS_G])
        expd = sb("expd", [P, G, BLOCKS, COL_TILES])
        weighed = sb("weighed", [P, G, BLOCKS, COL_TILES])
        neg_max = sb("neg_max", [P, G])
        den = sb("den", [P, G])
        num = sb("num", [P, G])
        inv = sb("inv", [P, G])
        pooled = sb("pooled", [P, T])
        feats = sb("feats", [P, T, N_DENSE])
        feats_w = sb("feats_w", [P, T, N_DENSE])
        linear = sb("linear", [P, T])
        linear_b = sb("linear_b", [P, T])
        logit = sb("logit", [P, T])
        decay = sb("decay", [P, T])
        decay1 = sb("decay1", [P, T])
        prob = sb("prob", [P, T])

        turned = [psum(f"turned{i}", [P, P]) for i in range(2)]
        first = [psum(f"first{i}", [P, PAIRS_C * P]) for i in range(3)]
        sums = [psum(f"sums{i}", [P, PAIRS_C * P]) for i in range(2)]
        back = psum("back", [P, PAIRS_C, P])

        ids_in = sem("ids_in")
        offsets_in = sem("offsets_in")
        par_in = sem("par_in")
        feats_in = sem("feats_in")
        rows_made = sem("rows_made")
        rows_ready = sem("rows_ready")
        steps_let_go = sem("steps_let_go")
        gathered = [sem(f"gathered{k}") for k in range(SLOTS)]
        w_ready = sem("w_ready")
        transposed = sem("transposed")
        emb_copied = sem("emb_copied")
        pieces_done = sem("pieces_done")
        first_done = sem("first_done")
        relu_done = sem("relu_done")
        sums_done = sem("sums_done")
        second_done = sem("second_done")
        back_done = sem("back_done")
        result_done = sem("result_done")
        max_done = sem("max_done")
        exp_done = sem("exp_done")
        num_done = sem("num_done")
        inv_done = sem("inv_done")
        pooled_done = sem("pooled_done")
        linear_steps = sem("linear_steps")
        logit_done = sem("logit_done")
        decay_done = sem("decay_done")
        decay1_done = sem("decay1_done")
        prob_done = sem("prob_done")
        masked = sem("masked")
        stored = sem("stored")

        block = ctx.enter_context(nc.Block())

        @block.sync
        def _(sp):
            sp.dma_start(ids[:], sparse.rearrange("(p t) f -> p t f", t=T)).then_inc(ids_in, 16)
            sp.dma_start(feats[:], dense.rearrange("(p t) n -> p t n", t=T)).then_inc(feats_in, 16)
            sp.wait_ge(prob_done, 1)
            sp.dma_start(out.rearrange("(p t) -> p t", t=T), prob[:]).then_inc(stored, 16)
            sp.wait_ge(stored, 16)

        @block.gpsimd
        def _(pool):
            stacked = tables.rearrange("f v d -> (f v) d")
            with pool.Fori(0, CYCLES) as c:
                for k in range(SLOTS):
                    pool.wait_ge(rows_ready, c * SLOTS + (k + 1))
                    pool.sem_inc(steps_let_go, 1)
                    for g in range(G):
                        pool.indirect_dma_start(
                            emb[:, k, g * D:(g + 1) * D], None, stacked,
                            bass.IndirectOffsetOnAxis(ap=row_slot[:, k, g:g + 1], axis=0),
                        ).then_inc(gathered[k], 16)

        @block.tensor
        def _(pe):
            ident = par[:, cols["ident"]]
            d_sel = par[:, cols["d"]].rearrange("p (e r) -> p e r", e=2)
            pe.wait_ge(par_in, 16)
            pe.wait_ge(w_ready, 1)
            with pe.Fori(0, QUADS) as q:

                def transpose_step(f):
                    pe.wait_ge(gathered[f % SLOTS], (q * (F // SLOTS) + (f // SLOTS + 1)) * (16 * G))
                    if f >= 2:
                        pe.wait_ge(emb_copied, q * F + (f - 1))
                        pe.wait_ge(pieces_done, q * PIECES + pieces_before_field(f - 1))
                    nc.tensor.transpose(turned[f % 2][:], emb[:, f % SLOTS, :], ident).then_inc(transposed, 1)

                def first_products(gr):
                    pe.wait_ge(pieces_done, q * PIECES + pieces_through_group(gr))
                    if gr >= 3:
                        pe.wait_ge(relu_done, q * GROUPS + (gr - 2))
                    for j in range(COL_TILES):
                        mm = nc.tensor.matmul(first[gr % 3][j * ROWS_C:(j + 1) * ROWS_C, :], w_block[:],
                                              ring[:, gr % RING, j * PAIRS_C:(j + 1) * PAIRS_C, :],
                                              start=True, stop=True)
                    mm.then_inc(first_done, 1)

                def second_products(gr):
                    n, c = gr // GROUPS_B, gr % GROUPS_B // 2
                    pe.wait_ge(relu_done, q * GROUPS + (gr + 1))
                    if gr % GROUPS_B == 0 and n >= 2:
                        pe.wait_ge(second_done, q * BANKS + (n - 1))
                    nc.tensor.matmul(sums[n % 2][32 * c:32 * (c + 1), :], d_sel[:, gr % 2, :],
                                     hidden[:, gr % 3, :], start=gr % 2 == 0,
                                     stop=gr % 2 == 1 or gr == GROUPS - 1).then_inc(sums_done, 1)

                def transpose_back(n):
                    pe.wait_ge(second_done, q * BANKS + (n + 1))
                    if n:
                        pe.wait_ge(result_done, q * BANKS + n)
                    for k in range(PAIRS_C):
                        mm = nc.tensor.transpose(back[:, k, :], second[:, n % 2, k * P:(k + 1) * P], ident)
                    mm.then_inc(back_done, 1)

                transpose_step(0)
                transpose_step(1)
                for f in range(1, F):
                    done = groups_of(f)
                    for gr in done:
                        if gr == done[-1] and f + 1 < F:
                            transpose_step(f + 1)
                        first_products(gr)
                        if gr >= 1:
                            second_products(gr - 1)
                        if gr >= GROUPS_B and gr % GROUPS_B == 2:
                            transpose_back(gr // GROUPS_B - 1)
                    if not done and f + 1 < F:
                        transpose_step(f + 1)
                second_products(GROUPS - 1)
                transpose_back(FULL - 1)
                transpose_back(FULL)

        @block.scalar
        def _(act):
            act.dma_start(par[:, cols["offset"]], params[:, cols["offset"]]).then_inc(offsets_in, 16)
            rest = slice(cols["offset"].stop, params.shape[1])
            act.dma_start(par[:, rest], params[:, rest]).then_inc(par_in, 16)
            act.wait_ge(par_in, 16)
            with act.Fori(0, QUADS) as q:

                def copy_step(f):
                    act.wait_ge(transposed, q * F + (f + 1))
                    nc.scalar.activation(emb_t[:, f, :], turned[f % 2][:], ACT.Copy).then_inc(emb_copied, 1)

                def relu_group(gr):
                    act.wait_ge(first_done, q * GROUPS + (gr + 1))
                    if gr >= 3:
                        act.wait_ge(sums_done, q * GROUPS + (gr - 2))
                    nc.scalar.activation(hidden[:, gr % 3, :], first[gr % 3][:], ACT.Relu,
                                         bias=par[:, cols["bias_a"]]).then_inc(relu_done, 1)

                def copy_sums(n):
                    used = P if n < FULL else 32
                    act.wait_ge(sums_done, q * GROUPS + min((n + 1) * GROUPS_B, GROUPS))
                    if n >= 2:
                        act.wait_ge(back_done, q * BANKS + (n - 1))
                    nc.scalar.activation(second[0:used, n % 2, :], sums[n % 2][0:used, :], ACT.Identity,
                                         bias=par[0:used, cols["bias_s"]]).then_inc(second_done, 1)

                copy_step(0)
                copy_step(1)
                for f in range(1, F):
                    done = groups_of(f)
                    for gr in done:
                        if gr == done[-1] and f + 1 < F:
                            copy_step(f + 1)
                        relu_group(gr)
                        if gr >= GROUPS_B and gr % GROUPS_B == 1:
                            copy_sums(gr // GROUPS_B - 1)
                    if not done and f + 1 < F:
                        copy_step(f + 1)
                copy_sums(FULL - 1)
                copy_sums(FULL)
                scores = result[:].rearrange("p n (o g j) -> p o g n j", o=OUTS, g=G)
                act.wait_ge(max_done, q + 1)
                for g in range(G):
                    nc.scalar.activation(expd[:, g], scores[:, 0, g], ACT.Exp, bias=neg_max[:, g:g + 1],
                                         accum_out=den[:, g:g + 1]).then_inc(exp_done, 1)
            act.wait_ge(logit_done, 1)
            nc.scalar.activation(decay[:], logit[:], ACT.Exp, scale=-1.0).then_inc(decay_done, 1)

        @block.vector
        def _(dve):
            dve.wait_ge(ids_in, 16)
            nc.vector.tensor_scalar(clamped[:], ids[:], float(-V), float(V - 1), ALU.max, ALU.min).then_inc(rows_made, 1)
            dve.wait_ge(rows_made, 1)
            nc.vector.tensor_scalar(wrap[:], clamped[:], 0.0, float(V), ALU.is_lt, ALU.mult).then_inc(rows_made, 1)
            dve.wait_ge(rows_made, 2)
            nc.vector.tensor_tensor(wrapped[:], clamped[:], wrap[:], ALU.add).then_inc(rows_made, 1)
            dve.wait_ge(rows_made, 3)
            dve.wait_ge(offsets_in, 16)
            by_step = wrapped[:].rearrange("p (q g) f -> p q f g", g=G)
            offset = par[:, cols["offset"]].unsqueeze(2).broadcast_to((P, F, G))
            nc.vector.tensor_tensor(row_slot[:], by_step[:, 0, 0:SLOTS, :], offset[:, 0:SLOTS, :],
                                    ALU.add).then_inc(rows_ready, SLOTS)
            for q in range(QUADS):
                nc.vector.tensor_tensor(rows[:, q * F:(q + 1) * F, :], by_step[:, q], offset, ALU.add).then_inc(rows_made, 1)
            nc.vector.memset(rows[:, STEPS:STEPS + SLOTS, :], 0).then_inc(rows_made, 1)

            dve.wait_ge(par_in, 16)
            nc.vector.tensor_tensor(w_block[:], par[:, cols["w"]], par[:, cols["sign"]], ALU.mult).then_inc(w_ready, 1)
            unused = result[:, BLOCKS - PAIRS_C + 1:BLOCKS, :].rearrange("p n (o g j) -> p n o g j", o=OUTS, g=G)
            nc.vector.memset(unused[:, :, 0, :, 1], MASKED).then_inc(masked, 1)
            nc.vector.memset(unused[:, :, 1, :, 1], 0.0).then_inc(masked, 1)
            dve.wait_ge(feats_in, 16)
            dense_w = par[:, cols["dense_w"]].unsqueeze(1).broadcast_to((P, T, N_DENSE))
            nc.vector.tensor_tensor(feats_w[:], feats[:], dense_w, ALU.mult).then_inc(linear_steps, 1)
            dve.wait_ge(linear_steps, 1)
            nc.vector.tensor_reduce(linear[:], feats_w[:], AX.X, ALU.add).then_inc(linear_steps, 1)
            dve.wait_ge(linear_steps, 2)
            nc.vector.tensor_scalar(linear_b[:], linear[:], par[:, cols["fin_b"]], None, ALU.add).then_inc(linear_steps, 1)
            dve.wait_ge(rows_made, 3 + QUADS + 1)
            dve.wait_ge(masked, 2)

            with dve.Fori(0, QUADS) as q:

                def pair_products(f, a, b):
                    gr, at = a // PAIRS_G, a % PAIRS_G
                    i = a - f * (f - 1) // 2
                    n = b - a
                    if at == 0 and gr >= RING:
                        dve.wait_ge(first_done, q * GROUPS + (gr - RING + 1))
                    nc.vector.tensor_tensor(ring[:, gr % RING, at:at + n, :], emb_t[:, i:i + n, :],
                                            turned[f % 2][:].unsqueeze(1).broadcast_to((P, n, P)),
                                            ALU.mult).then_inc(pieces_done, 1)

                def copy_back(n):
                    dve.wait_ge(back_done, q * BANKS + (n + 1))
                    if n < FULL:
                        blocks = PAIRS_C * GROUPS_B
                        nc.vector.tensor_copy(result[:, n * blocks:(n + 1) * blocks, :],
                                              back[:].rearrange("p k (e r) -> p (k e) r", r=ROWS_G)).then_inc(result_done, 1)
                    else:
                        to = result[:, BLOCKS - PAIRS_C:BLOCKS, :].rearrange("p n (r j) -> p n r j", j=COL_TILES)
                        fro = back[:, :, 0:ROWS_G].rearrange("p k (r j) -> p k r j", j=COL_TILES)
                        nc.vector.tensor_copy(to[:, 0, :, 1], fro[:, 0, :, 1])
                        nc.vector.tensor_copy(to[:, :, :, 0], fro[:, :, :, 0]).then_inc(result_done, 1)

                backs = 0
                for f in range(F):
                    dve.wait_ge(transposed, q * F + (f + 1))
                    nc.vector.tensor_copy(row_slot[:, f % SLOTS, :],
                                          rows[:, bass.ds(q * F + (f + SLOTS), 1), :]).then_inc(rows_ready, 1)
                    dve.wait_ge(emb_copied, q * F + (f + 1))
                    for field, a, b in pieces:
                        if field == f:
                            pair_products(f, a, b)
                    if f < F - 1 and f * (f + 1) // 2 // PAIRS_G - 4 >= (backs + 1) * GROUPS_B:
                        copy_back(backs)
                        backs += 1
                for n in range(backs, BANKS):
                    copy_back(n)

                scores = result[:].rearrange("p n (o g j) -> p o g n j", o=OUTS, g=G)
                dve.wait_ge(result_done, (q + 1) * BANKS)
                nc.vector.tensor_reduce(neg_max[:], scores[:, 0], AX.XY, ALU.max, negate=True).then_inc(max_done, 1)
                for g in range(G):
                    dve.wait_ge(exp_done, q * G + (g + 1))
                    nc.vector.tensor_tensor_reduce(out=weighed[:, g], in0=expd[:, g], in1=scores[:, 1, g], scale=1.0,
                                                   scalar=0.0, op0=ALU.mult, op1=ALU.add,
                                                   accum_out=num[:, g:g + 1]).then_inc(num_done, 1)
                nc.vector.reciprocal(inv[:], den[:]).then_inc(inv_done, 1)
                dve.wait_ge(num_done, (q + 1) * G)
                dve.wait_ge(inv_done, q + 1)
                nc.vector.tensor_tensor(pooled[:, bass.ds(q * G, G)], num[:], inv[:], ALU.mult).then_inc(pooled_done, 1)

            dve.wait_ge(pooled_done, QUADS)
            dve.wait_ge(linear_steps, 3)
            nc.vector.tensor_tensor(logit[:], pooled[:], linear_b[:], ALU.add).then_inc(logit_done, 1)
            dve.wait_ge(decay_done, 1)
            nc.vector.tensor_scalar(decay1[:], decay[:], 1.0, None, ALU.add).then_inc(decay1_done, 1)
            dve.wait_ge(decay1_done, 1)
            nc.vector.reciprocal(prob[:], decay1[:]).then_inc(prob_done, 1)


def lay_out_params(att_w, att_b, att_d, att_d_b, fin_w, fin_b, n_fields, vocab):
    import numpy as np

    D, H = att_w.shape
    n_dense = fin_w.shape[0] - D
    chans = H + 2
    cols, width = layout(n_fields, D, H, n_dense)
    par = np.zeros((P, width), np.float32)
    par[:, cols["offset"]] = np.arange(n_fields) * vocab
    w, sign = par[:, cols["w"]], par[:, cols["sign"]]
    d = np.zeros((P, 2, 32), np.float32)
    bias_a, bias_s = par[:, cols["bias_a"]], par[:, cols["bias_s"]]
    sign[:] = 1.0
    for g in range(G):
        c = g * chans
        w[g * D:(g + 1) * D, c:c + H] = att_w
        w[g * D:(g + 1) * D, c + H:c + H + 1] = fin_w[:D]
        w[g * D:(g + 1) * D, c + H + 1:c + H + 2] = fin_w[:D]
        sign[:, c + H + 1] = -1.0
        for j in range(COL_TILES):
            r = j * ROWS_C + c
            bias_a[r:r + H, 0] = att_b
            for e in range(2):
                score = e * ROWS_G + g * COL_TILES + j
                final = score + G * COL_TILES
                d[r:r + H, e, score] = att_d[:, 0]
                d[r + H, e, final] = 1.0
                d[r + H + 1, e, final] = -1.0
    par[:, cols["d"]] = d.reshape(P, -1)
    for group in range(GROUPS_B):
        bias_s[group * ROWS_G:group * ROWS_G + G * COL_TILES, 0] = att_d_b
    par[:, cols["dense_w"]] = fin_w[D:, 0]
    par[:, cols["fin_b"]] = fin_b
    par[:, cols["ident"]] = np.eye(P)
    return par


def kernel(r_dense, r_sparse, L0_rec_embed_tables, L0_rec_att_w_w, L0_rec_att_w_b, L0_rec_att_d_w,
           L0_rec_att_d_b, L0_rec_fin_w, L0_rec_fin_b):
    import numpy as np
    import concourse.bacc as bacc
    from concourse.bass_utils import run_bass_kernel_spmd

    tables = np.ascontiguousarray(L0_rec_embed_tables)
    arrays = {
        "dense": np.ascontiguousarray(r_dense),
        "sparse": np.ascontiguousarray(r_sparse),
        "tables": tables,
        "params": lay_out_params(np.asarray(L0_rec_att_w_w), np.asarray(L0_rec_att_w_b), np.asarray(L0_rec_att_d_w),
                                 np.asarray(L0_rec_att_d_b), np.asarray(L0_rec_fin_w), np.asarray(L0_rec_fin_b),
                                 tables.shape[0], tables.shape[1]),
    }
    nc = bacc.Bacc("TRN2", target_bir_lowering=False, num_devices=1)
    args = [nc.dram_tensor(name, a.shape, mybir.dt.from_np(a.dtype), kind="ExternalInput").ap()
            for name, a in arrays.items()]
    out = nc.dram_tensor("out", (arrays["dense"].shape[0],), mybir.dt.float32, kind="ExternalOutput").ap()
    attention_fm(nc, *args, out)
    return run_bass_kernel_spmd(nc, [arrays], core_ids=[0]).results[0]["out"]
```

```python
from contextlib import ExitStack

import concourse.bass as bass
from concourse import mybir

P = 128
G = 4
COL_TILES = 2
PAIRS_C = 4
PAIRS_G = COL_TILES * PAIRS_C
ROWS_C = P // COL_TILES
OUTS = 2
ROWS_G = OUTS * G * COL_TILES
GROUPS_B = P // ROWS_G
RING = 16
SLOTS = 13
HIDDEN = 4
MASKED = -3.0e38


def layout(n_fields, n_dense):
    at, cols = 0, {}
    for name, width in (("offset", n_fields), ("w", ROWS_C), ("sign", ROWS_C), ("d", 2 * 32), ("bias_a", 1),
                        ("bias_s", 1), ("dense_w", n_dense), ("fin_b", 1), ("ident", P)):
        cols[name] = slice(at, at + width)
        at += width
    return cols, at


def attention_fm(nc, dense, sparse, tables, params, out):
    f32, i32 = mybir.dt.float32, mybir.dt.int32
    ALU, ACT, AX = mybir.AluOpType, mybir.ActivationFunctionType, mybir.AxisListType

    B, F = sparse.shape
    V, D = tables.shape[1:]
    N_DENSE = dense.shape[1]
    T = B // P
    QUADS = T // G
    STEPS = QUADS * F
    CYCLES = STEPS // SLOTS
    PAIRS = F * (F - 1) // 2
    GROUPS = -(-PAIRS // PAIRS_G)
    BANKS = -(-GROUPS // GROUPS_B)
    FULL = BANKS - 1
    LAST = PAIRS - (GROUPS - 1) * PAIRS_G
    LAST_C = -(-LAST // COL_TILES)
    BLOCKS_B = PAIRS_C * GROUPS_B
    BLOCKS = FULL * BLOCKS_B + LAST_C
    EARLY = 3
    EARLY_BLOCKS = EARLY * BLOCKS_B
    assert G * D == P and B % (P * G) == 0 and F % SLOTS == 0 and GROUPS == FULL * GROUPS_B + 1
    assert LAST % COL_TILES == 1 and RING < GROUPS and EARLY < FULL

    pieces = []
    for f in range(F):
        a, end = f * (f - 1) // 2, f * (f + 1) // 2
        while a < end:
            b = min(end, (a // PAIRS_G + 1) * PAIRS_G)
            pieces.append((f, a, b))
            a = b
    PIECES = len(pieces)

    def pieces_before_field(f):
        return sum(1 for piece in pieces if piece[0] < f)

    def pieces_through_group(g):
        return sum(1 for piece in pieces if piece[1] < (g + 1) * PAIRS_G)

    def groups_of(f):
        first, end = f * (f - 1) // 2 // PAIRS_G, f * (f + 1) // 2 // PAIRS_G
        return list(range(first, GROUPS if f == F - 1 else end)) if f else []

    AHEAD = 1
    BACK_LAG = 3
    EARLY_FIELD = 1 + next(f for f in range(F) if f * (f + 1) // 2 // PAIRS_G >= EARLY * GROUPS_B + BACK_LAG)
    ROWS_MADE = 2 * 3 + QUADS + 1

    def pairs_c(gr):
        return PAIRS_C if gr < GROUPS - 1 else LAST_C

    cols, _ = layout(F, N_DENSE)

    ctx = ExitStack()
    with ctx:
        def sb(name, shape, dt=f32):
            return ctx.enter_context(nc.sbuf_tensor(name, shape, dt))

        def psum(name, shape):
            return ctx.enter_context(nc.psum_tensor(name, shape, f32))

        def sem(name):
            return ctx.enter_context(nc.semaphore(name))

        par = sb("par", [P, params.shape[1]])
        ids = sb("ids", [P, T, F], i32)
        clamped = sb("clamped", [P, T, F])
        wrap = sb("wrap", [P, T, F])
        moved = sb("moved", [P, T, F])
        rows = sb("rows", [P, STEPS + SLOTS, G], i32)
        row_slot = sb("row_slot", [P, SLOTS, G], i32)
        emb = sb("emb", [P, SLOTS, G * D])
        emb_t = sb("emb_t", [P, F, P])
        ring = sb("ring", [P, RING, PAIRS_C, COL_TILES, P])
        w_block = sb("w_block", [P, ROWS_C])
        hidden = sb("hidden", [P, HIDDEN, PAIRS_C * P])
        second = sb("second", [P, 2, PAIRS_C * P])
        result = sb("result", [P, BLOCKS, ROWS_G])
        expd = sb("expd", [P, G, BLOCKS, COL_TILES])
        weighed = sb("weighed", [P, G, BLOCKS, COL_TILES])
        neg_max = sb("neg_max", [P, G])
        neg_max_early = sb("neg_max_early", [P, G])
        neg_max_late = sb("neg_max_late", [P, G])
        rise = sb("rise", [P, G])
        fade = sb("fade", [P, G])
        early = sb("early", [P, 2, G])
        late = sb("late", [P, 2, G])
        faded = sb("faded", [P, 2, G])
        total = sb("total", [P, 2, G])
        inv = sb("inv", [P, G])
        pooled = sb("pooled", [P, T])
        feats = sb("feats", [P, T, N_DENSE])
        feats_w = sb("feats_w", [P, T, N_DENSE])
        linear = sb("linear", [P, T])
        linear_b = sb("linear_b", [P, T])
        logit = sb("logit", [P, T])
        decay = sb("decay", [P, T])
        decay1 = sb("decay1", [P, T])
        prob = sb("prob", [P, T])

        turned = [psum(f"turned{i}", [P, P]) for i in range(2)]
        first = [psum(f"first{i}", [P, PAIRS_C * P]) for i in range(2)]
        sums = [psum(f"sums{i}", [P, PAIRS_C * P]) for i in range(2)]
        back = [psum(f"back{i}", [P, PAIRS_C, P]) for i in range(2)]

        ids_in = sem("ids_in")
        offsets_in = sem("offsets_in")
        par_in = sem("par_in")
        feats_in = sem("feats_in")
        rows_made = sem("rows_made")
        rows_ready = sem("rows_ready")
        steps_let_go = sem("steps_let_go")
        gathered = [sem(f"gathered{k}") for k in range(SLOTS)]
        w_ready = sem("w_ready")
        transposed = sem("transposed")
        emb_copied = sem("emb_copied")
        pieces_done = sem("pieces_done")
        first_done = sem("first_done")
        relu_done = sem("relu_done")
        sums_done = sem("sums_done")
        second_done = sem("second_done")
        back_done = sem("back_done")
        result_done = sem("result_done")
        result_end_done = sem("result_end_done")
        early_max_done = sem("early_max_done")
        early_exp_done = sem("early_exp_done")
        early_num_done = sem("early_num_done")
        late_max_done = sem("late_max_done")
        max_done = sem("max_done")
        rise_done = sem("rise_done")
        fade_done = sem("fade_done")
        late_exp_done = sem("late_exp_done")
        late_num_done = sem("late_num_done")
        faded_done = sem("faded_done")
        total_done = sem("total_done")
        inv_done = sem("inv_done")
        pooled_done = sem("pooled_done")
        linear_steps = sem("linear_steps")
        logit_done = sem("logit_done")
        decay_done = sem("decay_done")
        decay1_done = sem("decay1_done")
        prob_done = sem("prob_done")
        masked = sem("masked")
        stored = sem("stored")

        block = ctx.enter_context(nc.Block())

        @block.sync
        def _(sp):
            sp.dma_start(ids[:], sparse.rearrange("(p t) f -> p t f", t=T)).then_inc(ids_in, 16)
            sp.dma_start(feats[:], dense.rearrange("(p t) n -> p t n", t=T)).then_inc(feats_in, 16)
            sp.wait_ge(prob_done, 1)
            sp.dma_start(out.rearrange("(p t) -> p t", t=T), prob[:]).then_inc(stored, 16)
            sp.wait_ge(stored, 16)

        @block.gpsimd
        def _(pool):
            stacked = tables.rearrange("f v d -> (f v) d")
            with pool.Fori(0, CYCLES) as c:
                for k in range(SLOTS):
                    pool.wait_ge(rows_ready, c * SLOTS + (k + 1))
                    pool.sem_inc(steps_let_go, 1)
                    for g in range(G):
                        pool.indirect_dma_start(
                            emb[:, k, g * D:(g + 1) * D], None, stacked,
                            bass.IndirectOffsetOnAxis(ap=row_slot[:, k, g:g + 1], axis=0),
                        ).then_inc(gathered[k], 16)

        @block.tensor
        def _(pe):
            ident = par[:, cols["ident"]]
            d_sel = par[:, cols["d"]].rearrange("p (e r) -> p e r", e=2)
            pe.wait_ge(par_in, 16)
            pe.wait_ge(w_ready, 1)
            with pe.Fori(0, QUADS) as q:

                def transpose_step(f):
                    pe.wait_ge(gathered[f % SLOTS], (q * (F // SLOTS) + (f // SLOTS + 1)) * (16 * G))
                    if f >= 2:
                        pe.wait_ge(emb_copied, q * F + (f - 1))
                        pe.wait_ge(pieces_done, q * PIECES + pieces_before_field(f - 1))
                    nc.tensor.transpose(turned[f % 2][:], emb[:, f % SLOTS, :], ident).then_inc(transposed, 1)

                def first_products(gr):
                    pe.wait_ge(pieces_done, q * PIECES + pieces_through_group(gr))
                    if gr >= 2:
                        pe.wait_ge(relu_done, q * GROUPS + (gr - 1))
                    n = pairs_c(gr)
                    for j in range(COL_TILES):
                        mm = nc.tensor.matmul(first[gr % 2][j * ROWS_C:(j + 1) * ROWS_C, 0:n * P], w_block[:],
                                              ring[:, gr % RING, 0:n, j, :], start=True, stop=True)
                    mm.then_inc(first_done, 1)

                def second_products(gr):
                    n, c = gr // GROUPS_B, gr % GROUPS_B // 2
                    pe.wait_ge(relu_done, q * GROUPS + (gr + 1))
                    if gr % GROUPS_B == 0 and n >= 2:
                        pe.wait_ge(second_done, q * BANKS + (n - 1))
                    cut = slice(0, pairs_c(gr) * P)
                    nc.tensor.matmul(sums[n % 2][32 * c:32 * (c + 1), cut], d_sel[:, gr % 2, :],
                                     hidden[:, gr % HIDDEN, cut], start=gr % 2 == 0,
                                     stop=gr % 2 == 1 or gr == GROUPS - 1).then_inc(sums_done, 1)

                def transpose_back(n):
                    pe.wait_ge(second_done, q * BANKS + (n + 1))
                    if n >= 2:
                        pe.wait_ge(result_done, q * (BANKS - 2) + (n - 1))
                    for k in range(PAIRS_C if n < FULL else LAST_C):
                        mm = nc.tensor.transpose(back[n % 2][:, k, :], second[:, n % 2, k * P:(k + 1) * P], ident)
                    mm.then_inc(back_done, 1)

                transpose_step(0)
                transpose_step(1)
                for f in range(1, F):
                    done = groups_of(f)
                    for gr in done:
                        if gr == done[-AHEAD:][0] and f + 1 < F:
                            transpose_step(f + 1)
                        first_products(gr)
                        if gr >= 2:
                            second_products(gr - 2)
                        if gr >= GROUPS_B and gr % GROUPS_B == 2:
                            transpose_back(gr // GROUPS_B - 1)
                    if not done and f + 1 < F:
                        transpose_step(f + 1)
                second_products(GROUPS - 2)
                second_products(GROUPS - 1)
                transpose_back(FULL - 1)
                transpose_back(FULL)

        @block.scalar
        def _(act):
            act.dma_start(par[:, cols["offset"]], params[:, cols["offset"]]).then_inc(offsets_in, 16)
            rest = slice(cols["offset"].stop, params.shape[1])
            act.dma_start(par[:, rest], params[:, rest]).then_inc(par_in, 16)
            scores = result[:].rearrange("p n (o g j) -> p o g n j", o=OUTS, g=G)
            act.wait_ge(par_in, 16)
            act.wait_ge(rows_made, ROWS_MADE)
            with act.Fori(0, QUADS) as q:

                def copy_step(f):
                    act.wait_ge(transposed, q * F + (f + 1))
                    nc.scalar.activation(emb_t[:, f, :], turned[f % 2][:], ACT.Copy).then_inc(emb_copied, 1)
                    nc.scalar.activation(row_slot[:, f % SLOTS, :], rows[:, bass.ds(q * F + (f + SLOTS), 1), :],
                                         ACT.Copy).then_inc(rows_ready, 1)

                def relu_group(gr):
                    act.wait_ge(first_done, q * GROUPS + (gr + 1))
                    if gr >= HIDDEN:
                        act.wait_ge(sums_done, q * GROUPS + (gr - HIDDEN + 1))
                    cut = slice(0, pairs_c(gr) * P)
                    nc.scalar.activation(hidden[:, gr % HIDDEN, cut], first[gr % 2][:, cut], ACT.Relu,
                                         bias=par[:, cols["bias_a"]]).then_inc(relu_done, 1)

                def copy_sums(n):
                    used, cut = (P, PAIRS_C * P) if n < FULL else (32, LAST_C * P)
                    act.wait_ge(sums_done, q * GROUPS + min((n + 1) * GROUPS_B, GROUPS))
                    if n >= 2:
                        act.wait_ge(back_done, q * BANKS + (n - 1))
                    nc.scalar.activation(second[0:used, n % 2, 0:cut], sums[n % 2][0:used, 0:cut], ACT.Identity,
                                         bias=par[0:used, cols["bias_s"]]).then_inc(second_done, 1)

                def copy_back(n):
                    act.wait_ge(back_done, q * BANKS + (n + 1))
                    nc.scalar.activation(result[:, n * BLOCKS_B:(n + 1) * BLOCKS_B, :],
                                         back[n % 2][:].rearrange("p k (e r) -> p (k e) r", r=ROWS_G),
                                         ACT.Copy).then_inc(result_done, 1)

                def exponentiate_early(g0, g1):
                    act.wait_ge(early_max_done, q + 1)
                    for g in range(g0, g1):
                        nc.scalar.activation(expd[:, g, 0:EARLY_BLOCKS], scores[:, 0, g, 0:EARLY_BLOCKS], ACT.Exp,
                                             bias=neg_max_early[:, g:g + 1],
                                             accum_out=early[:, 0, g:g + 1]).then_inc(early_exp_done, 1)

                copy_step(0)
                copy_step(1)
                for f in range(1, F):
                    done = groups_of(f)
                    for gr in done:
                        if gr == done[-AHEAD:][0] and f + 1 < F:
                            copy_step(f + 1)
                        relu_group(gr)
                        if gr >= GROUPS_B and gr % GROUPS_B == 1:
                            copy_sums(gr // GROUPS_B - 1)
                        if gr >= GROUPS_B and gr % GROUPS_B == 3:
                            copy_back(gr // GROUPS_B - 1)
                    if not done and f + 1 < F:
                        copy_step(f + 1)
                    if f == EARLY_FIELD + 1:
                        exponentiate_early(0, G // 2)
                    if f == EARLY_FIELD + 2:
                        exponentiate_early(G // 2, G)
                copy_sums(FULL - 1)
                copy_sums(FULL)
                act.wait_ge(max_done, q + 1)
                for g in range(G):
                    nc.scalar.activation(expd[:, g, EARLY_BLOCKS:], scores[:, 0, g, EARLY_BLOCKS:], ACT.Exp,
                                         bias=neg_max[:, g:g + 1],
                                         accum_out=late[:, 0, g:g + 1]).then_inc(late_exp_done, 1)
                    if g == 1:
                        act.wait_ge(rise_done, q + 1)
                        nc.scalar.activation(fade[:], rise[:], ACT.Exp).then_inc(fade_done, 1)
            act.wait_ge(logit_done, 1)
            nc.scalar.activation(decay[:], logit[:], ACT.Exp, scale=-1.0).then_inc(decay_done, 1)

        @block.vector
        def _(dve):
            dve.wait_ge(ids_in, 16)
            dve.wait_ge(offsets_in, 16)
            by_step = "p (q g) f -> p q f g"
            made = 0
            for t, f in ((G, SLOTS), (T, F)):
                nc.vector.tensor_scalar(clamped[:, 0:t, 0:f], ids[:, 0:t, 0:f], float(-V), float(V - 1),
                                        ALU.max, ALU.min).then_inc(rows_made, 1)
                dve.wait_ge(rows_made, made + 1)
                nc.vector.tensor_scalar(wrap[:, 0:t, 0:f], clamped[:, 0:t, 0:f], 0.0, float(V),
                                        ALU.is_lt, ALU.mult).then_inc(rows_made, 1)
                offset = par[:, cols["offset"]][:, 0:f].unsqueeze(1).broadcast_to((P, t, f))
                nc.vector.tensor_tensor(moved[:, 0:t, 0:f], clamped[:, 0:t, 0:f], offset, ALU.add).then_inc(rows_made, 1)
                dve.wait_ge(rows_made, made + 3)
                made += 3
                if t == G:
                    nc.vector.tensor_tensor(row_slot[:].rearrange("p f g -> p g f"), moved[:, 0:t, 0:f],
                                            wrap[:, 0:t, 0:f], ALU.add).then_inc(rows_ready, SLOTS)
                    dve.wait_ge(rows_ready, SLOTS)
            for q in range(QUADS):
                nc.vector.tensor_tensor(rows[:, q * F:(q + 1) * F, :], moved[:].rearrange(by_step, g=G)[:, q],
                                        wrap[:].rearrange(by_step, g=G)[:, q], ALU.add).then_inc(rows_made, 1)
            nc.vector.memset(rows[:, STEPS:STEPS + SLOTS, :], 0).then_inc(rows_made, 1)

            dve.wait_ge(par_in, 16)
            nc.vector.tensor_tensor(w_block[:], par[:, cols["w"]], par[:, cols["sign"]], ALU.mult).then_inc(w_ready, 1)
            unused = result[:, BLOCKS - 1, :].rearrange("p (o g j) -> p o g j", o=OUTS, g=G)
            nc.vector.memset(unused[:, 0, :, 1], MASKED).then_inc(masked, 1)
            nc.vector.memset(unused[:, 1, :, 1], 0.0).then_inc(masked, 1)
            dve.wait_ge(feats_in, 16)
            dense_w = par[:, cols["dense_w"]].unsqueeze(1).broadcast_to((P, T, N_DENSE))
            nc.vector.tensor_tensor(feats_w[:], feats[:], dense_w, ALU.mult).then_inc(linear_steps, 1)
            dve.wait_ge(linear_steps, 1)
            nc.vector.tensor_reduce(linear[:], feats_w[:], AX.X, ALU.add).then_inc(linear_steps, 1)
            dve.wait_ge(linear_steps, 2)
            nc.vector.tensor_scalar(linear_b[:], linear[:], par[:, cols["fin_b"]], None, ALU.add).then_inc(linear_steps, 1)
            dve.wait_ge(rows_made, ROWS_MADE)
            dve.wait_ge(masked, 2)

            scores = result[:].rearrange("p n (o g j) -> p o g n j", o=OUTS, g=G)
            with dve.Fori(0, QUADS) as q:

                def pair_products(f, a, b):
                    gr, at = a // PAIRS_G, a % PAIRS_G
                    i = a - f * (f - 1) // 2
                    n = b - a
                    if at == 0 and gr >= RING:
                        dve.wait_ge(first_done, q * GROUPS + (gr - RING + 1))
                    slot = ring[:, gr % RING].rearrange("p c j b -> p (c j) b")
                    nc.vector.tensor_tensor(slot[:, at:at + n, :], emb_t[:, i:i + n, :],
                                            turned[f % 2][:].unsqueeze(1).broadcast_to((P, n, P)),
                                            ALU.mult).then_inc(pieces_done, 1)

                def weigh_early(g):
                    dve.wait_ge(early_exp_done, q * G + (g + 1))
                    nc.vector.tensor_tensor_reduce(
                        out=weighed[:, g, 0:EARLY_BLOCKS], in0=expd[:, g, 0:EARLY_BLOCKS],
                        in1=scores[:, 1, g, 0:EARLY_BLOCKS], scale=1.0, scalar=0.0, op0=ALU.mult, op1=ALU.add,
                        accum_out=early[:, 1, g:g + 1]).then_inc(early_num_done, 1)

                for f in range(F):
                    dve.wait_ge(emb_copied, q * F + (f + 1))
                    for field, a, b in pieces:
                        if field == f:
                            pair_products(f, a, b)
                    if f == EARLY_FIELD:
                        dve.wait_ge(result_done, q * (BANKS - 2) + EARLY)
                        nc.vector.tensor_reduce(neg_max_early[:], scores[:, 0, :, 0:EARLY_BLOCKS], AX.XY, ALU.max,
                                                negate=True).then_inc(early_max_done, 1)
                for g in range(G):
                    weigh_early(g)
                one = "p (r j) -> p r j"
                dve.wait_ge(back_done, q * BANKS + FULL)
                nc.vector.tensor_copy(result[:, (FULL - 1) * BLOCKS_B:FULL * BLOCKS_B, :],
                                      back[(FULL - 1) % 2][:].rearrange("p k (e r) -> p (k e) r", r=ROWS_G)
                                      ).then_inc(result_end_done, 1)
                dve.wait_ge(back_done, q * BANKS + BANKS)
                end = result[:, FULL * BLOCKS_B:, :]
                nc.vector.tensor_copy(end[:, 0:LAST_C - 1], back[FULL % 2][:, 0:LAST_C - 1, 0:ROWS_G])
                nc.vector.tensor_copy(end[:, LAST_C - 1].rearrange(one, j=COL_TILES)[:, :, 0],
                                      back[FULL % 2][:, LAST_C - 1, 0:ROWS_G].rearrange(one, j=COL_TILES)[:, :, 0]
                                      ).then_inc(result_end_done, 1)

                dve.wait_ge(result_done, (q + 1) * (BANKS - 2))
                dve.wait_ge(result_end_done, (q + 1) * 2)
                nc.vector.tensor_reduce(neg_max_late[:], scores[:, 0, :, EARLY_BLOCKS:], AX.XY, ALU.max,
                                        negate=True).then_inc(late_max_done, 1)
                dve.wait_ge(late_max_done, q + 1)
                dve.wait_ge(early_max_done, q + 1)
                nc.vector.tensor_tensor(neg_max[:], neg_max_early[:], neg_max_late[:], ALU.min).then_inc(max_done, 1)
                dve.wait_ge(max_done, q + 1)
                nc.vector.tensor_tensor(rise[:], neg_max[:], neg_max_early[:], ALU.subtract).then_inc(rise_done, 1)
                for g in range(G):
                    dve.wait_ge(late_exp_done, q * G + (g + 1))
                    if g == G - 1:
                        dve.wait_ge(faded_done, q + 1)
                        nc.vector.tensor_tensor(total[:, 0], faded[:, 0], late[:, 0], ALU.add).then_inc(total_done, 1)
                    nc.vector.tensor_tensor_reduce(
                        out=weighed[:, g, EARLY_BLOCKS:], in0=expd[:, g, EARLY_BLOCKS:],
                        in1=scores[:, 1, g, EARLY_BLOCKS:], scale=1.0, scalar=0.0, op0=ALU.mult, op1=ALU.add,
                        accum_out=late[:, 1, g:g + 1]).then_inc(late_num_done, 1)
                    if g == 1:
                        dve.wait_ge(fade_done, q + 1)
                        dve.wait_ge(early_num_done, (q + 1) * G)
                        nc.vector.tensor_tensor(faded[:], early[:], fade[:].unsqueeze(1).broadcast_to((P, 2, G)),
                                                ALU.mult).then_inc(faded_done, 1)
                dve.wait_ge(total_done, q * 2 + 1)
                nc.vector.reciprocal(inv[:], total[:, 0]).then_inc(inv_done, 1)
                dve.wait_ge(late_num_done, (q + 1) * G)
                nc.vector.tensor_tensor(total[:, 1], faded[:, 1], late[:, 1], ALU.add).then_inc(total_done, 1)
                dve.wait_ge(total_done, (q + 1) * 2)
                dve.wait_ge(inv_done, q + 1)
                nc.vector.tensor_tensor(pooled[:, bass.ds(q * G, G)], total[:, 1], inv[:], ALU.mult).then_inc(pooled_done, 1)

            dve.wait_ge(pooled_done, QUADS)
            dve.wait_ge(linear_steps, 3)
            nc.vector.tensor_tensor(logit[:], pooled[:], linear_b[:], ALU.add).then_inc(logit_done, 1)
            dve.wait_ge(decay_done, 1)
            nc.vector.tensor_scalar(decay1[:], decay[:], 1.0, None, ALU.add).then_inc(decay1_done, 1)
            dve.wait_ge(decay1_done, 1)
            nc.vector.reciprocal(prob[:], decay1[:]).then_inc(prob_done, 1)


def lay_out_params(att_w, att_b, att_d, att_d_b, fin_w, fin_b, n_fields, vocab):
    import numpy as np

    D, H = att_w.shape
    n_dense = fin_w.shape[0] - D
    chans = H + 2
    cols, width = layout(n_fields, n_dense)
    par = np.zeros((P, width), np.float32)
    par[:, cols["offset"]] = np.arange(n_fields) * vocab
    w, sign = par[:, cols["w"]], par[:, cols["sign"]]
    d = np.zeros((P, 2, 32), np.float32)
    bias_a, bias_s = par[:, cols["bias_a"]], par[:, cols["bias_s"]]
    sign[:] = 1.0
    for g in range(G):
        c = g * chans
        w[g * D:(g + 1) * D, c:c + H] = att_w
        w[g * D:(g + 1) * D, c + H:c + H + 1] = fin_w[:D]
        w[g * D:(g + 1) * D, c + H + 1:c + H + 2] = fin_w[:D]
        sign[:, c + H + 1] = -1.0
        for j in range(COL_TILES):
            r = j * ROWS_C + c
            bias_a[r:r + H, 0] = att_b
            for e in range(2):
                score = e * ROWS_G + g * COL_TILES + j
                final = score + G * COL_TILES
                d[r:r + H, e, score] = att_d[:, 0]
                d[r + H, e, final] = 1.0
                d[r + H + 1, e, final] = -1.0
    par[:, cols["d"]] = d.reshape(P, -1)
    for group in range(GROUPS_B):
        bias_s[group * ROWS_G:group * ROWS_G + G * COL_TILES, 0] = att_d_b
    par[:, cols["dense_w"]] = fin_w[D:, 0]
    par[:, cols["fin_b"]] = fin_b
    par[:, cols["ident"]] = np.eye(P)
    return par


def kernel(r_dense, r_sparse, L0_rec_embed_tables, L0_rec_att_w_w, L0_rec_att_w_b, L0_rec_att_d_w,
           L0_rec_att_d_b, L0_rec_fin_w, L0_rec_fin_b):
    import numpy as np
    import concourse.bacc as bacc
    from concourse.bass_utils import run_bass_kernel_spmd

    tables = np.ascontiguousarray(L0_rec_embed_tables)
    arrays = {
        "dense": np.ascontiguousarray(r_dense),
        "sparse": np.ascontiguousarray(r_sparse),
        "tables": tables,
        "params": lay_out_params(np.asarray(L0_rec_att_w_w), np.asarray(L0_rec_att_w_b), np.asarray(L0_rec_att_d_w),
                                 np.asarray(L0_rec_att_d_b), np.asarray(L0_rec_fin_w), np.asarray(L0_rec_fin_b),
                                 tables.shape[0], tables.shape[1]),
    }
    nc = bacc.Bacc("TRN2", target_bir_lowering=False, num_devices=1)
    args = [nc.dram_tensor(name, a.shape, mybir.dt.from_np(a.dtype), kind="ExternalInput").ap()
            for name, a in arrays.items()]
    out = nc.dram_tensor("out", (arrays["dense"].shape[0],), mybir.dt.float32, kind="ExternalOutput").ap()
    attention_fm(nc, *args, out)
    return run_bass_kernel_spmd(nc, [arrays], core_ids=[0]).results[0]["out"]
```
